# Optimizing a Trainium2 kernel written in Bass

```python
import numpy as np
import jax
import jax.numpy as jnp

def _softmax(x, axis=-1):
    return jax.nn.softmax(x, axis=axis)

def _gelu(x):
    return jax.nn.gelu(x, approximate=True)

def _silu(x):
    return jax.nn.silu(x)

def _sigmoid(x):
    return jax.nn.sigmoid(x)

def _layernorm(x, axis=-1, eps=1e-05):
    m = jnp.mean(x, axis=axis, keepdims=True)
    v = jnp.var(x, axis=axis, keepdims=True)
    return (x - m) / jnp.sqrt(v + eps)

def _scatter_add(tgt, idx, src, axis=0):
    return tgt.at[idx].add(src)

def _segment_sum(src, seg, n):
    return jax.ops.segment_sum(src, seg, n)
kernel_name = 'mk_adj_seq_d1_adj_r2_72eec5'

def setup_inputs(seed: int=0):
    np.random.seed(seed)
    _w = jnp.asarray

    def _rec_inputs():
        import jax
        import jax.numpy as jnp
        _gk = jax.random.key(seed)
        x = -0.0005207 + 1.001 * jax.random.normal(jax.random.fold_in(_gk, 1), (128, 128, 256), jnp.float32)
        _a = jax.random.bernoulli(jax.random.fold_in(_gk, 2), 0.0625, (128, 128, 128))
        _a = jnp.logical_or(_a, jnp.eye(128, dtype=bool))
        adj = _a.astype(jnp.int32)
        return (x, adj)
    x, adj = _rec_inputs()

    def _L0_gnn_setup():
        import jax, jax.numpy as jnp
        import numpy as np
        B, S, D, H = (2, 1024, 256, 8)
        HD = D // H
        EPS = 1e-05

        def _ln(x, g, b):
            mu = jnp.mean(x, axis=-1, keepdims=True)
            var = jnp.mean((x - mu) ** 2, axis=-1, keepdims=True)
            return (x - mu) * jax.lax.rsqrt(var + EPS) * g + b
        key = jax.random.key(seed)
        ks = jax.random.split(key, 16)
        x = jax.random.normal(ks[0], (B, S, D), dtype=jnp.float32)
        adj = jax.random.randint(ks[1], (B, S, S), 0, 2, dtype=jnp.int32)
        adj = adj.at[:, jnp.arange(S), jnp.arange(S)].set(1)
        edge_attr = jax.random.normal(ks[2], (B, S, S), dtype=jnp.float32)
        sc = 1.0 / np.sqrt(D)
        p = lambda k, shp: jax.random.normal(k, shp, dtype=jnp.float32) * sc
        return {'x': x, 'adj_matrix': adj, 'edge_attr_matrix': edge_attr, 'ln1_g': jnp.ones((D,)), 'ln1_b': jnp.zeros((D,)), 'ln2_g': jnp.ones((D,)), 'ln2_b': jnp.zeros((D,)), 'wq': p(ks[3], (D, D)), 'bq': jnp.zeros((D,)), 'wk': p(ks[4], (D, D)), 'bk': jnp.zeros((D,)), 'wv': p(ks[5], (D, D)), 'bv': jnp.zeros((D,)), 'wo': p(ks[6], (D, D)), 'bo': jnp.zeros((D,)), 'w1': p(ks[7], (D, 4 * D)), 'b1': jnp.zeros((4 * D,)), 'w2': p(ks[8], (4 * D, D)), 'b2': jnp.zeros((D,))}
    _L0_gnn_all = _L0_gnn_setup()
    _L0_gnn_in = {k: v for k, v in _L0_gnn_all.items() if k in ('ln1_g', 'ln1_b', 'ln2_g', 'ln2_b', 'wq', 'bq', 'wk', 'bk', 'wv', 'bv', 'wo', 'bo', 'w1', 'b1', 'w2', 'b2')}
    del _L0_gnn_all
    return {'x': x, 'adj': adj, 'L0_gnn_ln1_g': _L0_gnn_in['ln1_g'], 'L0_gnn_ln1_b': _L0_gnn_in['ln1_b'], 'L0_gnn_ln2_g': _L0_gnn_in['ln2_g'], 'L0_gnn_ln2_b': _L0_gnn_in['ln2_b'], 'L0_gnn_wq': _L0_gnn_in['wq'], 'L0_gnn_bq': _L0_gnn_in['bq'], 'L0_gnn_wk': _L0_gnn_in['wk'], 'L0_gnn_bk': _L0_gnn_in['bk'], 'L0_gnn_wv': _L0_gnn_in['wv'], 'L0_gnn_bv': _L0_gnn_in['bv'], 'L0_gnn_wo': _L0_gnn_in['wo'], 'L0_gnn_bo': _L0_gnn_in['bo'], 'L0_gnn_w1': _L0_gnn_in['w1'], 'L0_gnn_b1': _L0_gnn_in['b1'], 'L0_gnn_w2': _L0_gnn_in['w2'], 'L0_gnn_b2': _L0_gnn_in['b2']}

def reference(x, adj, L0_gnn_ln1_g, L0_gnn_ln1_b, L0_gnn_ln2_g, L0_gnn_ln2_b, L0_gnn_wq, L0_gnn_bq, L0_gnn_wk, L0_gnn_bk, L0_gnn_wv, L0_gnn_bv, L0_gnn_wo, L0_gnn_bo, L0_gnn_w1, L0_gnn_b1, L0_gnn_w2, L0_gnn_b2):
    import jax
    import jax.numpy as jnp

    def _L0_gnn_ref(x, adj_matrix, edge_attr_matrix, ln1_g, ln1_b, ln2_g, ln2_b, wq, bq, wk, bk, wv, bv, wo, bo, w1, b1, w2, b2):
        import jax, jax.numpy as jnp
        import numpy as np
        B, S, D, H = (2, 1024, 256, 8)
        HD = D // H
        EPS = 1e-05

        def _ln(x, g, b):
            mu = jnp.mean(x, axis=-1, keepdims=True)
            var = jnp.mean((x - mu) ** 2, axis=-1, keepdims=True)
            return (x - mu) * jax.lax.rsqrt(var + EPS) * g + b
        b, s, d = x.shape
        residual = x
        nx = _ln(x, ln1_g, ln1_b)
        q = (nx @ wq + bq).reshape(b, s, H, HD).transpose(0, 2, 1, 3)
        k = (nx @ wk + bk).reshape(b, s, H, HD).transpose(0, 2, 1, 3)
        v = (nx @ wv + bv).reshape(b, s, H, HD).transpose(0, 2, 1, 3)
        adjf = adj_matrix.astype(jnp.float32)
        bias = jnp.where(adj_matrix > 0, 0.1 * edge_attr_matrix * adjf, -jnp.inf)[:, None]
        scores = jnp.einsum('bhqd,bhkd->bhqk', q, k) / np.sqrt(HD) + bias
        attn = jax.nn.softmax(scores, axis=-1)
        out = jnp.einsum('bhqk,bhkd->bhqd', attn, v)
        out = out.transpose(0, 2, 1, 3).reshape(b, s, d)
        x1 = residual + (out @ wo + bo)
        n2 = _ln(x1, ln2_g, ln2_b)
        mlp = jax.nn.gelu(n2 @ w1 + b1, approximate=False) @ w2 + b2
        return x1 + mlp
    x = _L0_gnn_ref(x, adj, adj, L0_gnn_ln1_g, L0_gnn_ln1_b, L0_gnn_ln2_g, L0_gnn_ln2_b, L0_gnn_wq, L0_gnn_bq, L0_gnn_wk, L0_gnn_bk, L0_gnn_wv, L0_gnn_bv, L0_gnn_wo, L0_gnn_bo, L0_gnn_w1, L0_gnn_b1, L0_gnn_w2, L0_gnn_b2)
    return x

_drawn_inputs = setup_inputs


def setup_inputs(seed=0):
    import zlib

    import numpy as np

    out = dict(_drawn_inputs(seed))
    spreads = {'L0_gnn_ln1_g': (1.0, 0.2),
     'L0_gnn_ln1_b': (0.0, 0.1),
     'L0_gnn_ln2_g': (1.0, 0.2),
     'L0_gnn_ln2_b': (0.0, 0.1),
     'L0_gnn_bq': (0.0, 0.1),
     'L0_gnn_bk': (0.0, 0.1),
     'L0_gnn_bv': (0.0, 0.1),
     'L0_gnn_bo': (0.0, 0.1),
     'L0_gnn_b1': (0.0, 0.1),
     'L0_gnn_b2': (0.0, 0.1)}
    factors = {}
    for name, (base, spread) in spreads.items():
        noise = np.random.default_rng([zlib.crc32(name.encode()), seed]).standard_normal(out[name].shape)
        drawn = base * np.exp(spread * noise) if base else spread * noise
        out[name] = jnp.asarray(drawn.astype(out[name].dtype))
    for name, factor in factors.items():
        out[name] = (out[name] * factor).astype(out[name].dtype)
    return out
```

```python
from contextlib import ExitStack

import numpy as np
import concourse.bass as bass
from concourse import mybir

F32 = mybir.dt.float32
F32R = mybir.dt.float32r
I32 = mybir.dt.int32
ALU = mybir.AluOpType
ACT = mybir.ActivationFunctionType
AX = mybir.AxisListType

P = 128
GB = 4
D = 256
DC = D // P
H = 8
HD = D // H
F = 1024
FC = F // P
RPB = P // HD
TOK = GB * P
VW = HD + 1
SCALE = 1.0 / float(np.sqrt(HD))
EPS = 1e-5
MASKED = -1e30

UNITS = ([("down", 0, -2), ("down", 1, -2)]
         + [("down", 2, -2), ("down", 3, -2)]
         + [("qk", 0, 1), ("qk", 1, 1), ("qk", 2, 1), ("qk", 3, 1)]
         + [("v", 0, 1), ("v", 1, 1)] + [("up", m, -1) for m in range(FC)])
PLACE = {(kind, i): at for at, (kind, i, _) in enumerate(UNITS)}
PER_GROUP = {"down": GB, "v": 2, "qk": 4, "up": FC}
assert len(UNITS) % 2 == 0


def bank_of(kind, i):
    return PLACE[(kind, i)] % 2


HEAD_ORDER = [0, 4, 1, 5, 2, 6, 3, 7]
HEAD_BANK = {h: (h % RPB) % 2 for h in range(H)}
HEAD_COL = {0: 0, 4: 1, 2: 2, 6: 3, 1: 0, 5: 1, 3: 2, 7: 3}


def head_place(h):
    return HEAD_BANK[h] * 4 + HEAD_COL[h]


class Step:

    def __init__(self, n, half, parity, groups, steady):
        self.n, self.half, self.parity, self.groups, self.steady = n, half, parity, groups, steady

    def has(self, off):
        return self.steady or 0 <= self.n + off < self.groups

    def parity_of(self, off):
        return (self.parity + off) % 2

    def has_graph(self, slot, back):
        return self.steady or 0 <= GB * self.n + slot - back < GB * self.groups

    def graphs(self, slot, back):
        return self.n * GB + (slot - back + 1)

    def count(self, off, per, i):
        return self.n * per + (off * per + i + 1)

    def loads(self, off):
        return self.half * 16 + ((self.parity + off) // 2 * 16 + 16)

    def positive(self, off, per, i):
        return self.steady or self.count(off, per, i) > 0


def steps(eng, groups, body):
    first, last = 2, groups - 2
    for n in range(-1, first):
        body(Step(n, n // 2, n % 2, groups, False))
    with eng.Fori(first // 2, last // 2) as i:
        for u in range(2):
            body(Step(i * 2 + u, i, u, groups, True))
    for n in range(last, groups + 2):
        body(Step(n, n // 2, n % 2, groups, False))


def gnn_block(nc, x, adj, cols, wq, wk, wv, wo, bo, w1, w2, b2, out):
    groups = x.shape[0] // GB
    assert x.shape[1] == P and x.shape[2] == D and groups % 2 == 0 and groups >= 6

    with ExitStack() as ctx:
        def sb(name, shape, dt=F32):
            return ctx.enter_context(nc.sbuf_tensor(name, shape, dt))

        def ps(name, shape):
            return ctx.enter_context(nc.psum_tensor(name, shape, F32))

        def sem(name):
            return ctx.enter_context(nc.semaphore(name))

        wa_hi = sb("wa_hi", [P, 4, DC, D], F32R)
        wa_lo = sb("wa_lo", [P, 4, DC, D], F32R)
        w1_hi = sb("w1_hi", [P, DC, F], F32R)
        w1_lo = sb("w1_lo", [P, DC, F], F32R)
        w2_hi = sb("w2_hi", [P, FC, D], F32R)
        w2_lo = sb("w2_lo", [P, FC, D], F32R)
        ident = sb("ident", [P, P])
        cols_in = sb("cols_in", [P, 7 * DC + FC])
        ln_cols = cols_in[:, 0:4 * DC].rearrange("p (j c) -> p j c", c=DC)
        bias_in = cols_in[:, 4 * DC:7 * DC].rearrange("p (j c) -> p j c", c=DC)
        b1_in = cols_in[:, 7 * DC:7 * DC + FC]
        bias_col = sb("bias_col", [P, 3, DC])
        bq_scaled = sb("bq_scaled", [P, DC])
        b1_col = sb("b1_col", [P, FC])
        bv_wide = sb("bv_wide", [P, DC, P])
        bo_rows = sb("bo_rows", [P, D])
        b2_rows = sb("b2_rows", [P, D])

        xin = sb("xin", [P, 2, GB, D])
        x1 = sb("x1", [P, 2, GB, D])
        res = sb("res", [P, 2, GB, D])
        xhat = sb("xhat", [P, GB, D])
        nhat = sb("nhat", [P, GB, D])
        xt_hi = sb("xt_hi", [P, DC, TOK], F32R)
        xt_lo = sb("xt_lo", [P, DC, TOK], F32R)
        nt_hi = sb("nt_hi", [P, DC, TOK], F32R)
        nt_lo = sb("nt_lo", [P, DC, TOK], F32R)
        qk = sb("qk", [P, 2, 4, TOK])
        vals = sb("vals", [P, 2, GB, H, VW])
        adj_in = sb("adj_in", [P, 2, GB, P], I32)
        ebias = sb("ebias", [P, 2, GB, P])
        absent = sb("absent", [P, GB, P])
        adjf = sb("adjf", [P, GB, P])
        tenth = sb("tenth", [P, GB, P])
        sraw = sb("sraw", [P, H, P])
        prob = sb("prob", [P, H, P])
        probt = sb("probt", [P, H, P])
        rmax = sb("rmax", [P, H])
        rsum = sb("rsum", [P, H])
        attn = sb("attn", [P, D])
        at_hi = sb("at_hi", [P, DC, P], F32R)
        at_lo = sb("at_lo", [P, DC, P], F32R)
        hid = sb("hid", [P, 3, TOK])
        hid_hi = sb("hid_hi", [P, FC, TOK], F32R)
        hid_lo = sb("hid_lo", [P, FC, TOK], F32R)
        st1 = sb("st1", [P, GB, 6])
        st2 = sb("st2", [P, GB, 6])
        mv1 = sb("mv1", [P, GB, 2])
        mv2 = sb("mv2", [P, GB, 2])
        ve1 = sb("ve1", [P, GB])
        ve2 = sb("ve2", [P, GB])
        rstd1 = sb("rstd1", [P, GB])
        rstd2 = sb("rstd2", [P, GB])
        mhalf = sb("mhalf", [P, GB])
        eps = sb("eps", [P, GB])
        gate = sb("gate", [P, 1])
        w1_raw = qk[:, 0, :, :].rearrange("p c n -> p (c n)").rearrange("p (c n) -> p c n", c=DC)
        w2_raw = qk[:, 1, :, :].rearrange("p c n -> p (c n)").rearrange("p (c n) -> p c n", c=FC)
        wa_raw = x1[:, :, :, :].rearrange("p a b n -> p (a b) n").rearrange(
            "p (a b) n -> p a b n", a=4)

        scores = ps("scores", [P, 2, 512])
        turned = ps("turned", [P, 2, 512])
        work = ps("work", [P, 2, 512])
        mixed = ps("mixed", [P, 512])
        wout = ps("wout", [P, 512])

        x_loaded = [sem("x_loaded0"), sem("x_loaded1")]
        adj_loaded = [sem("adj_loaded0"), sem("adj_loaded1")]
        stored = [sem("stored0"), sem("stored1")]
        cols_loaded = sem("cols_loaded")
        wa_loaded = sem("wa_loaded")
        w1_loaded = sem("w1_loaded")
        w2_loaded = sem("w2_loaded")
        rows_loaded = sem("rows_loaded")
        ident_clear = sem("ident_clear")
        ident_ready = sem("ident_ready")
        ones_set = sem("ones_set")
        mhalf_set = sem("mhalf_set")
        hi_made = sem("hi_made")
        lo_made = sem("lo_made")
        cols_ready = sem("cols_ready")
        cols_added = sem("cols_added")
        q_scaled = sem("q_scaled")
        bv_spread = sem("bv_spread")
        bo_ready = sem("bo_ready")
        bo_added = sem("bo_added")
        full = {k: sem(f"{k}_full") for k in (*PER_GROUP, "xt", "nt")}
        hi_taken = {k: sem(f"{k}_hi_taken") for k in ("xt", "nt")}
        taken = {k: sem(f"{k}_taken") for k in (*PER_GROUP, "xt", "nt")}
        x_stats = sem("x_stats")
        x_stat1 = sem("x_stat1")
        x_veps = sem("x_veps")
        x_rstd = sem("x_rstd")
        xhat_ready = sem("xhat_ready")
        n_stat1 = sem("n_stat1")
        n_stats = sem("n_stats")
        n_veps = sem("n_veps")
        n_rstd = sem("n_rstd")
        nhat_ready = sem("nhat_ready")
        x1_ready = sem("x1_ready")
        x1_summed = sem("x1_summed")
        res_ready = sem("res_ready")
        absent_ready = sem("absent_ready")
        adjf_ready = sem("adjf_ready")
        tenth_ready = sem("tenth_ready")
        square_ready = sem("square_ready")
        ebias_ready = sem("ebias_ready")
        scores_full = sem("scores_full")
        scores_taken = sem("scores_taken")
        max_ready = sem("max_ready")
        shifted = sem("shifted")
        prob_ready = sem("prob_ready")
        turned_full = sem("turned_full")
        turned_taken = sem("turned_taken")
        mixed_full = sem("mixed_full")
        sum_inverted = sem("sum_inverted")
        attn_ready = sem("attn_ready")
        at_full = sem("at_full")
        at_hi_taken = sem("at_hi_taken")
        at_taken = sem("at_taken")
        wout_full = sem("wout_full")
        hid_ready = sem("hid_ready")
        hid_hi_ready = sem("hid_hi_ready")
        hid_lo_ready = sem("hid_lo_ready")

        x_g = x.rearrange("(g b) s d -> g s b d", b=GB)
        adj_g = adj.rearrange("(g b) q k -> g q b k", b=GB)
        out_g = out.rearrange("(g b) s d -> g s b d", b=GB)

        block = ctx.enter_context(nc.Block())

        @block.sync
        def _(sp):
            def group(step, off):
                return sp.snap(step.n + off) if step.steady else step.n + off

            def load(step, off, guard):
                if not step.has(off):
                    return
                par = step.parity_of(off)
                x_src, adj_src = x_g[group(step, off)], adj_g[group(step, off)]
                if guard:
                    sp.wait_ge(x1_ready, step.count(off - 2, 1, 0))
                sp.dma_start(xin[:, par, :, :], x_src).then_inc(x_loaded[par], 16)
                if guard:
                    sp.wait_ge(ebias_ready, step.count(off - 2, 1, 0))
                sp.dma_start(adj_in[:, par, :, :], adj_src).then_inc(adj_loaded[par], 16)

            start = Step(0, 0, 0, groups, False)
            load(start, 0, False)
            chunked = "(c p) n -> p c n"
            sp.dma_start(cols_in[:, :], cols).then_inc(cols_loaded, 16)
            for j, w in enumerate((wq, wk, wv, wo)):
                sp.dma_start(wa_raw[:, j, :, :], w.rearrange(chunked, p=P)).then_inc(wa_loaded, 16)
            sp.dma_start(w1_raw, w1.rearrange(chunked, p=P)).then_inc(w1_loaded, 16)
            sp.dma_start(w2_raw, w2.rearrange(chunked, p=P)).then_inc(w2_loaded, 16)
            sp.dma_start(bo_rows[:, :], bo.rearrange("(a n) -> a n", a=1).to_broadcast([P, D])).then_inc(rows_loaded, 16)
            sp.dma_start(b2_rows[:, :], b2.rearrange("(a n) -> a n", a=1).to_broadcast([P, D])).then_inc(rows_loaded, 16)
            load(start, 1, False)

            def store(step, b):
                if step.has(-2):
                    par = step.parity_of(-2)
                    dst = out_g[group(step, -2)][:, b, :]
                    sp.wait_ge(taken["down"], step.count(-2, GB, b))
                    sp.dma_start(dst, res[:, par, b, :]).then_inc(stored[par], 16)

            def body(step):
                store(step, 0)
                store(step, 1)
                if step.has(0):
                    load(step, 2, True)
                store(step, 2)
                store(step, 3)

            steps(sp, groups, body)
            for par in range(2):
                sp.wait_ge(stored[par], 16 * GB * (groups // 2))

        @block.tensor
        def _(pe):
            def free(step, kind, i):
                at = PLACE[(kind, i)] - 2
                back = 0
                while True:
                    if at < 0:
                        at += len(UNITS)
                        back += 1
                    k, j, off = UNITS[at]
                    if step.has(off - back):
                        pe.wait_ge(taken[k], step.count(off - back, PER_GROUP[k], j))
                        return
                    if not step.steady and step.n - back < -2:
                        return
                    at -= 2

            def three(o, lhs_hi, lhs_lo, rhs_hi, rhs_lo, first, last):
                pe.matmul(o, lhs_hi, rhs_hi, start=first, stop=False)
                pe.matmul(o, lhs_hi, rhs_lo, start=False, stop=False)
                return pe.matmul(o, lhs_lo, rhs_hi, start=False, stop=last)

            def column(o, w, off):
                for c in range(DC):
                    mm = pe.matmul(o, w[:, c, :], off[:, c:c + 1], start=(c == 0), stop=(c == DC - 1))
                return mm

            pe.wait_ge(cols_loaded, 16)
            pe.wait_ge(wa_loaded, 16 * 4)
            for j in range(3):
                for m in range(DC):
                    column(mixed[:, j * DC + m:j * DC + m + 1], wa_raw[:, j, :, m * P:(m + 1) * P],
                           ln_cols[:, 1, :])
            pe.wait_ge(w1_loaded, 16)
            for m in range(FC):
                mm = column(mixed[:, 3 * DC + m:3 * DC + m + 1], w1_raw[:, :, m * P:(m + 1) * P],
                            ln_cols[:, 3, :])
            mm.then_inc(cols_ready, 1)
            pe.wait_ge(bv_spread, 1)
            for c in range(DC):
                mm = pe.matmul(wout[:, 0:D], bv_wide[:, c, :], wa_raw[:, 3, c, :],
                               start=(c == 0), stop=(c == DC - 1))
            mm.then_inc(bo_ready, 1)
            pe.wait_ge(ident_ready, 1)
            pe.wait_ge(hi_made, 6)
            pe.wait_ge(lo_made, 6)
            pe.wait_ge(bo_added, 1)

            def score(step, s):
                if not step.has_graph(s, 0) or not step.has(0):
                    return
                par = step.parity_of(0)
                if s == 0:
                    pe.wait_ge(taken["qk"], step.count(0, 4, 3))
                if step.has_graph(s, 1):
                    pe.wait_ge(scores_taken, step.graphs(s, 1))
                cols = slice(s * P, (s + 1) * P)
                for at_head, h in enumerate(HEAD_ORDER):
                    r = slice(HD * (h % RPB), HD * (h % RPB) + HD)
                    at = HEAD_COL[h] * P
                    if at_head in (4, 6):
                        pe.wait_ge(scores_full, step.graphs(s, 1) * 4 + (at_head // 2 - 1))
                    mm = pe.matmul(scores[:, HEAD_BANK[h], at:at + P], qk[r, par, h // RPB, cols],
                                   qk[r, par, DC + h // RPB, cols], start=True, stop=True)
                    if at_head % 2 == 1:
                        mm.then_inc(scores_full, 1)

            def turn(step, s):
                if not step.has_graph(s, 1):
                    return
                pe.wait_ge(prob_ready, step.graphs(s, 1))
                if step.has_graph(s, 2):
                    pe.wait_ge(turned_taken, step.graphs(s, 2) * 2)
                for kind, slot, off in (("xt", 1, 1), ("nt", 2, -1)):
                    if s == slot + 1 and step.has(off):
                        pe.wait_ge(taken[kind], step.count(off, DC, DC - 1))
                for half in range(2):
                    for j in range(4):
                        mm = pe.transpose(turned[:, half, j * P:(j + 1) * P], prob[:, half * 4 + j, :],
                                          ident[:, :])
                    mm.then_inc(turned_full, 1)

            def mix(step, s):
                if not step.has_graph(s, 1):
                    return
                par = step.parity_of(-1 if s == 0 else 0)
                b = (s - 1) % GB
                pe.wait_ge(turned_taken, step.graphs(s, 1) * 2)
                if s == 1:
                    pe.wait_ge(taken["v"], step.count(0, 2, 1))
                if step.has_graph(s, 2):
                    pe.wait_ge(at_taken, step.graphs(s, 2))
                for h in range(H):
                    mm = pe.matmul(mixed[:, h * VW:(h + 1) * VW], probt[:, head_place(h), :],
                                   vals[:, par, b, h, :], start=True, stop=True)
                mm.then_inc(mixed_full, 1)

            def turn_attn(step, s):
                if not step.has_graph(s, 1):
                    return
                pe.wait_ge(attn_ready, step.graphs(s, 1))
                for c in range(DC):
                    mm = pe.transpose(mixed[:, c * P:(c + 1) * P], attn[:, c * P:(c + 1) * P], ident[:, :])
                mm.then_inc(at_full, 1)

            def project_out(step, s):
                if not step.has_graph(s, 2):
                    return
                pe.wait_ge(at_taken, step.graphs(s, 2))
                if step.has_graph(s, 3):
                    pe.wait_ge(x1_summed, step.graphs(s, 3))
                for c in range(DC):
                    mm = three(wout[:, 0:D], at_hi[:, c, :], at_lo[:, c, :], wa_hi[:, 3, c, :],
                               wa_lo[:, 3, c, :], c == 0, c == DC - 1)
                mm.then_inc(wout_full, 1)

            def flip(step, s, kind, c):
                off = 1 if kind == "xt" else -1
                if not step.has(off):
                    return
                src, ready = (xhat, xhat_ready) if kind == "xt" else (nhat, nhat_ready)
                if step.has_graph(s, 1):
                    pe.wait_ge(turned_taken, step.graphs(s, 1) * 2)
                for b in range(GB):
                    if c == 0:
                        pe.wait_ge(ready, step.count(off, GB, b))
                    mm = pe.transpose(turned[:, c, b * P:(b + 1) * P],
                                      src[:, b, c * P:(c + 1) * P], ident[:, :])
                mm.then_inc(full[kind], 1)

            def values(step, half):
                if not step.has(1):
                    return
                free(step, "v", half)
                for j in range(2):
                    cols = slice((half * 2 + j) * P, (half * 2 + j + 1) * P)
                    for c in range(DC):
                        mm = three(work[:, bank_of("v", half), j * D:(j + 1) * D], xt_hi[:, c, cols],
                                   xt_lo[:, c, cols], wa_hi[:, 2, c, :], wa_lo[:, 2, c, :],
                                   c == 0, c == DC - 1)
                mm.then_inc(full["v"], 1)

            def query_key(step, m):
                if not step.has(1):
                    return
                free(step, "qk", m)
                if m == 0:
                    pe.wait_ge(taken["xt"], step.count(1, DC, DC - 1))
                w, cols = m // DC, slice((m % DC) * P, (m % DC + 1) * P)
                for c in range(DC):
                    mm = three(work[:, bank_of("qk", m), :], wa_hi[:, w, c, cols], wa_lo[:, w, c, cols],
                               xt_hi[:, c, :], xt_lo[:, c, :], c == 0, c == DC - 1)
                mm.then_inc(full["qk"], 1)

            def up(step, m):
                if not step.has(-1):
                    return
                free(step, "up", m)
                if m == 0:
                    pe.wait_ge(taken["nt"], step.count(-1, DC, DC - 1))
                cols = slice(m * P, (m + 1) * P)
                for c in range(DC):
                    mm = three(work[:, bank_of("up", m), :], w1_hi[:, c, cols], w1_lo[:, c, cols],
                               nt_hi[:, c, :], nt_lo[:, c, :], c == 0, c == DC - 1)
                mm.then_inc(full["up"], 1)

            def down(step, b):
                if not step.has(-2):
                    return
                free(step, "down", b)
                if b == 0:
                    pe.wait_ge(hid_lo_ready, step.count(-2, FC, FC - 1))
                cols = slice(b * P, (b + 1) * P)
                for m in range(FC):
                    mm = three(work[:, bank_of("down", b), 0:D], hid_hi[:, m, cols], hid_lo[:, m, cols],
                               w2_hi[:, m, :], w2_lo[:, m, :], m == 0, m == FC - 1)
                mm.then_inc(full["down"], 1)

            def body(step):
                score(step, 0)
                turn(step, 0)
                down(step, 0)
                mix(step, 0)
                project_out(step, 0)
                down(step, 1)
                turn_attn(step, 0)
                score(step, 1)
                turn(step, 1)
                down(step, 2)
                mix(step, 1)
                project_out(step, 1)
                flip(step, 1, "xt", 0)
                flip(step, 1, "xt", 1)
                down(step, 3)
                turn_attn(step, 1)
                score(step, 2)
                turn(step, 2)
                query_key(step, 0)
                query_key(step, 1)
                mix(step, 2)
                project_out(step, 2)
                query_key(step, 2)
                query_key(step, 3)
                flip(step, 2, "nt", 0)
                flip(step, 2, "nt", 1)
                turn_attn(step, 2)
                score(step, 3)
                turn(step, 3)
                values(step, 0)
                mix(step, 3)
                project_out(step, 3)
                values(step, 1)
                for m in range(FC):
                    up(step, m)
                turn_attn(step, 3)

            steps(pe, groups, body)

        @block.scalar
        def _(act):
            act.wait_ge(cols_loaded, 16)
            act.wait_ge(wa_loaded, 16 * 4)
            for j in range(3):
                for c in range(DC):
                    a = act.activation(wa_hi[:, j, c, :], wa_raw[:, j, c, :], ACT.Copy,
                                       scale=ln_cols[:, 0, c:c + 1])
                a.then_inc(hi_made, 1)
            act.activation(wa_hi[:, 3, :, :], wa_raw[:, 3, :, :], ACT.Copy).then_inc(hi_made, 1)
            act.wait_ge(w1_loaded, 16)
            for c in range(DC):
                a = act.activation(w1_hi[:, c, :], w1_raw[:, c, :], ACT.Copy, scale=ln_cols[:, 2, c:c + 1])
            a.then_inc(hi_made, 1)
            act.wait_ge(w2_loaded, 16)
            act.activation(w2_hi[:, :, :], w2_raw, ACT.Copy).then_inc(hi_made, 1)
            act.wait_ge(q_scaled, 1)
            act.wait_ge(lo_made, 6)
            act.wait_ge(cols_added, 2)
            act.wait_ge(ones_set, 1)

            def turned_copy(step, s):
                if not step.has_graph(s, 1):
                    return
                for half in range(2):
                    act.wait_ge(turned_full, step.graphs(s, 1) * 2 + (half - 1))
                    act.activation(probt[:, half * 4:half * 4 + 4, :], turned[:, half, :].rearrange(
                        "p (h q) -> p h q", q=P), ACT.Copy).then_inc(turned_taken, 1)

            def exponential(step, s):
                if not step.has(0):
                    return
                act.wait_ge(shifted, step.graphs(s, 0))
                if step.has_graph(s, 1):
                    act.wait_ge(turned_full, step.graphs(s, 1) * 2)
                act.activation(prob[:, :, :], sraw[:, :, :], ACT.Exp).then_inc(prob_ready, 1)

            def attn_hi(step, s):
                if not step.has_graph(s, 1):
                    return
                act.wait_ge(at_full, step.graphs(s, 1))
                act.activation(at_hi[:, :, :], mixed[:, 0:D].rearrange("p (c q) -> p c q", c=DC),
                               ACT.Copy).then_inc(at_hi_taken, 1)

            def flip_hi(step, kind):
                off = 1 if kind == "xt" else -1
                if not step.has(off):
                    return
                dst = xt_hi if kind == "xt" else nt_hi
                for c in range(DC):
                    act.wait_ge(full[kind], step.count(off, DC, c))
                    act.activation(dst[:, c, :], turned[:, c, :], ACT.Copy)\
                       .then_inc(hi_taken[kind], 1)

            def values_copy(step, half):
                if not step.has(1):
                    return
                act.wait_ge(full["v"], step.count(1, 2, half))
                act.activation(
                    vals[:, step.parity_of(1), half * 2:half * 2 + 2, :, 0:HD],
                    work[:, bank_of("v", half), :].rearrange("p (b h d) -> p b h d", b=2, h=H),
                    ACT.Copy).then_inc(taken["v"], 1)

            def query_key_copy(step, m):
                if not step.has(1):
                    return
                act.wait_ge(full["qk"], step.count(1, 4, m))
                q = m < DC
                b = bq_scaled[:, m:m + 1] if q else bias_col[:, 1, m - DC:m - DC + 1]
                act.activation(qk[:, step.parity_of(1), m, :], work[:, bank_of("qk", m), :], ACT.Identity,
                               bias=b, scale=SCALE if q else 1.0).then_inc(taken["qk"], 1)

            def gelu(step, m):
                if not step.has(-1):
                    return
                if step.positive(-1, FC, max(m - 3, -1)):
                    act.wait_ge(hid_lo_ready, step.count(-1, FC, max(m - 3, -1)))
                act.wait_ge(full["up"], step.count(-1, FC, m))
                act.activation(hid[:, m % 3, :], work[:, bank_of("up", m), :], ACT.Gelu,
                               bias=b1_col[:, m:m + 1]).then_inc(taken["up"], 1)

            def hidden_hi(step, m):
                if not step.has(-1):
                    return
                act.wait_ge(taken["up"], step.count(-1, FC, m))
                act.activation(hid_hi[:, m, :], hid[:, m % 3, :], ACT.Copy).then_inc(hid_hi_ready, 1)

            def body(step):
                turned_copy(step, 0)
                exponential(step, 0)
                attn_hi(step, 0)
                turned_copy(step, 1)
                exponential(step, 1)
                flip_hi(step, "xt")
                attn_hi(step, 1)
                turned_copy(step, 2)
                query_key_copy(step, 0)
                exponential(step, 2)
                for m in range(1, 4):
                    query_key_copy(step, m)
                flip_hi(step, "nt")
                attn_hi(step, 2)
                turned_copy(step, 3)
                exponential(step, 3)
                values_copy(step, 0)
                values_copy(step, 1)
                for m in range(FC):
                    gelu(step, m)
                    if m >= 1:
                        hidden_hi(step, m - 1)
                hidden_hi(step, FC - 1)
                attn_hi(step, 3)

            steps(act, groups, body)

        @block.vector
        def _(dve):
            dve.memset(vals[:, :, :, :, HD:VW], 1.0).then_inc(ones_set, 1)
            dve.wait_ge(cols_loaded, 16)
            dve.wait_ge(wa_loaded, 16 * 4)
            for j in range(3):
                dve.wait_ge(hi_made, j + 1)
                for c in range(DC):
                    a = dve.scalar_tensor_tensor(wa_lo[:, j, c, :], wa_raw[:, j, c, :], ln_cols[:, 0, c:c + 1],
                                                 wa_hi[:, j, c, :].bitcast(F32), ALU.mult, ALU.subtract)
                a.then_inc(lo_made, 1)
            dve.wait_ge(hi_made, 4)
            dve.tensor_tensor(wa_lo[:, 3, :, :], wa_raw[:, 3, :, :], wa_hi[:, 3, :, :].bitcast(F32),
                              ALU.subtract).then_inc(lo_made, 1)
            dve.wait_ge(w1_loaded, 16)
            dve.wait_ge(hi_made, 5)
            for c in range(DC):
                a = dve.scalar_tensor_tensor(w1_lo[:, c, :], w1_raw[:, c, :], ln_cols[:, 2, c:c + 1],
                                             w1_hi[:, c, :].bitcast(F32), ALU.mult, ALU.subtract)
            a.then_inc(lo_made, 1)
            dve.wait_ge(w2_loaded, 16)
            dve.wait_ge(hi_made, 6)
            dve.tensor_tensor(w2_lo[:, :, :], w2_raw, w2_hi[:, :, :].bitcast(F32),
                              ALU.subtract).then_inc(lo_made, 1)
            dve.wait_ge(cols_ready, 1)
            dve.tensor_tensor(bias_col[:, :, :], mixed[:, 0:3 * DC].rearrange("p (j c) -> p j c", j=3),
                              bias_in, ALU.add).then_inc(cols_added, 1)
            dve.tensor_tensor(b1_col[:, :], mixed[:, 3 * DC:3 * DC + FC], b1_in,
                              ALU.add).then_inc(cols_added, 1)
            dve.wait_ge(cols_added, 2)
            dve.tensor_scalar(bq_scaled[:, :], bias_col[:, 0, :], SCALE, None, ALU.mult)\
               .then_inc(q_scaled, 1)
            dve.tensor_copy(bv_wide[:, :, :], bias_col[:, 2, :].rearrange("p (c a) -> p c a", a=1)
                            .to_broadcast([P, DC, P])).then_inc(bv_spread, 1)
            dve.wait_ge(rows_loaded, 32)
            dve.wait_ge(bo_ready, 1)
            dve.tensor_tensor(bo_rows[:, :], wout[:, 0:D], bo_rows[:, :], ALU.add).then_inc(bo_added, 1)

            def softmax(step, s):
                if not step.has(0):
                    return
                par = step.parity_of(0)
                dve.wait_ge(scores_full, step.graphs(s, 0) * 4)
                if s == 0:
                    dve.wait_ge(ebias_ready, step.count(0, 1, 0))
                if step.has_graph(s, 1):
                    dve.wait_ge(prob_ready, step.graphs(s, 1))
                edge = ebias[:, par, s, :].rearrange("p (a k) -> p a k", a=1).to_broadcast([P, H, P])
                dve.tensor_tensor(sraw[:, :, :], scores[:, :, :].rearrange("p t (h k) -> p (t h) k", k=P),
                                  edge, ALU.add).then_inc(scores_taken, 1)
                dve.wait_ge(scores_taken, step.graphs(s, 0))
                dve.tensor_reduce(rmax[:, :], sraw[:, :, :], AX.X, ALU.max).then_inc(max_ready, 1)
                dve.wait_ge(max_ready, step.graphs(s, 0))
                dve.tensor_tensor(sraw[:, :, :], sraw[:, :, :],
                                  rmax[:, :].rearrange("p (h a) -> p h a", a=1).to_broadcast([P, H, P]),
                                  ALU.subtract).then_inc(shifted, 1)

            def normalise(step, s):
                if not step.has_graph(s, 1):
                    return
                dve.wait_ge(mixed_full, step.graphs(s, 1))
                heads = mixed[:, 0:H * VW].rearrange("p (h d) -> p h d", d=VW)
                dve.reciprocal(rsum[:, :].rearrange("p (h a) -> p h a", a=1),
                               heads[:, :, HD:VW]).then_inc(sum_inverted, 1)
                dve.wait_ge(sum_inverted, step.graphs(s, 1))
                dve.tensor_tensor(attn[:, :].rearrange("p (h d) -> p h d", d=HD), heads[:, :, 0:HD],
                                  rsum[:, :].rearrange("p (h a) -> p h a", a=1).to_broadcast([P, H, HD]),
                                  ALU.mult).then_inc(attn_ready, 1)

            def attn_lo(step, s):
                if not step.has_graph(s, 1):
                    return
                dve.wait_ge(at_hi_taken, step.graphs(s, 1))
                dve.tensor_tensor(at_lo[:, :, :], mixed[:, 0:D].rearrange("p (c q) -> p c q", c=DC),
                                  at_hi[:, :, :].bitcast(F32), ALU.subtract).then_inc(at_taken, 1)

            def residual(step, s):
                if not step.has_graph(s, 2):
                    return
                b = (s - 2) % GB
                off = -1 if s < 2 else 0
                par = step.parity_of(off)
                if b == 0:
                    dve.wait_ge(x1_ready, step.count(off, 1, 0))
                dve.wait_ge(wout_full, step.graphs(s, 2))
                dve.tensor_tensor(x1[:, par, b, :], wout[:, 0:D], x1[:, par, b, :],
                                  ALU.add).then_inc(x1_summed, 1)
                dve.wait_ge(x1_summed, step.graphs(s, 2))
                dve.bn_stats(st2[:, b, :], x1[:, par, b, :]).then_inc(n_stat1, 1)
                if b == GB - 1:
                    dve.wait_ge(n_stat1, step.graphs(s, 2))
                    dve.memset(gate[:, :], 0.0)
                    for j in range(GB):
                        a = dve.bn_aggr(mv2[:, j, :], st2[:, j, :])
                    a.then_inc(n_stats, 1)

            def stats1(step):
                if not step.has(1):
                    return
                par = step.parity_of(1)
                dve.wait_ge(x_loaded[par], step.loads(1))
                for b in range(GB):
                    a = dve.bn_stats(st1[:, b, :], xin[:, par, b, :])
                a.then_inc(x_stat1, 1)
                dve.wait_ge(x_stat1, step.count(1, 1, 0))
                dve.memset(gate[:, :], 0.0)
                for b in range(GB):
                    a = dve.bn_aggr(mv1[:, b, :], st1[:, b, :])
                a.then_inc(x_stats, 1)

            def norm1(step):
                if not step.has(1):
                    return
                par = step.parity_of(1)
                dve.wait_ge(x_rstd, step.count(1, 1, 0))
                if step.positive(0, DC, DC - 1):
                    dve.wait_ge(full["xt"], step.count(0, DC, DC - 1))
                for b in range(GB):
                    dve.tensor_scalar(xhat[:, b, :], xin[:, par, b, :], mv1[:, b, 0:1], rstd1[:, b:b + 1],
                                      ALU.subtract, ALU.mult).then_inc(xhat_ready, 1)

            def norm2(step):
                if not step.has(-1):
                    return
                par = step.parity_of(-1)
                dve.wait_ge(n_rstd, step.count(-1, 1, 0))
                if step.positive(-2, DC, DC - 1):
                    dve.wait_ge(full["nt"], step.count(-2, DC, DC - 1))
                for b in range(GB):
                    dve.tensor_scalar(nhat[:, b, :], x1[:, par, b, :], mv2[:, b, 0:1], rstd2[:, b:b + 1],
                                      ALU.subtract, ALU.mult).then_inc(nhat_ready, 1)

            def flip_lo(step, kind):
                off = 1 if kind == "xt" else -1
                if not step.has(off):
                    return
                hi, lo = (xt_hi, xt_lo) if kind == "xt" else (nt_hi, nt_lo)
                for c in range(DC):
                    dve.wait_ge(hi_taken[kind], step.count(off, DC, c))
                    dve.tensor_tensor(lo[:, c, :], turned[:, c, :], hi[:, c, :].bitcast(F32),
                                      ALU.subtract).then_inc(taken[kind], 1)

            def hidden_lo(step, m):
                if not step.has(-1):
                    return
                dve.wait_ge(hid_hi_ready, step.count(-1, FC, m))
                dve.tensor_tensor(hid_lo[:, m, :], hid[:, m % 3, :], hid_hi[:, m, :].bitcast(F32),
                                  ALU.subtract).then_inc(hid_lo_ready, 1)

            def result(step, b):
                if not step.has(-2):
                    return
                par = step.parity_of(-2)
                if b == 0:
                    dve.wait_ge(res_ready, step.count(-2, 1, 0))
                dve.wait_ge(full["down"], step.count(-2, GB, b))
                dve.tensor_tensor(res[:, par, b, :], work[:, bank_of("down", b), 0:D],
                                  res[:, par, b, :], ALU.add).then_inc(taken["down"], 1)

            def body(step):
                softmax(step, 0)
                result(step, 0)
                normalise(step, 0)
                residual(step, 0)
                stats1(step)
                result(step, 1)
                norm1(step)
                attn_lo(step, 0)
                softmax(step, 1)
                result(step, 2)
                normalise(step, 1)
                residual(step, 1)
                flip_lo(step, "xt")
                result(step, 3)
                attn_lo(step, 1)
                softmax(step, 2)
                norm2(step)
                normalise(step, 2)
                residual(step, 2)
                flip_lo(step, "nt")
                attn_lo(step, 2)
                softmax(step, 3)
                normalise(step, 3)
                residual(step, 3)
                for m in range(FC):
                    hidden_lo(step, m)
                attn_lo(step, 3)

            steps(dve, groups, body)

        @block.gpsimd
        def _(pool):
            pool.memset(ident[:, :], 0.0).then_inc(ident_clear, 1)
            pool.wait_ge(ident_clear, 1)
            pool.affine_select(out=ident[:, :], in_=ident[:, :], compare_op=ALU.not_equal, fill=1.0,
                               base=0, pattern=[[-1, P]], channel_multiplier=1).then_inc(ident_ready, 1)
            pool.memset(mhalf[:, :], -0.5).then_inc(mhalf_set, 1)
            pool.memset(eps[:, :], EPS).then_inc(mhalf_set, 1)
            pool.wait_ge(mhalf_set, 2)

            def rstd(step, off, stats, mv, ve, veps, o, done):
                if not step.has(off):
                    return
                pool.wait_ge(stats, step.count(off, 1, 0))
                pool.tensor_tensor(ve[:, :], mv[:, :, 1:2].rearrange("p b a -> p (b a)"), eps[:, :],
                                   ALU.add).then_inc(veps, 1)
                pool.wait_ge(veps, step.count(off, 1, 0))
                pool.tensor_tensor(o[:, :], ve[:, :], mhalf[:, :], ALU.pow).then_inc(done, 1)

            def residual_start(step):
                if not step.has(0):
                    return
                par = step.parity_of(0)
                pool.wait_ge(x_loaded[par], step.loads(0))
                pool.wait_ge(xhat_ready, step.count(0, GB, GB - 1))
                if step.positive(-2, 1, 0):
                    pool.wait_ge(nhat_ready, step.count(-2, GB, GB - 1))
                    pool.wait_ge(res_ready, step.count(-2, 1, 0))
                pool.tensor_tensor(x1[:, par, :, :], xin[:, par, :, :],
                                   bo_rows[:, :].rearrange("p (a n) -> p a n", a=1).to_broadcast([P, GB, D]),
                                   ALU.add).then_inc(x1_ready, 1)

            def result_start(step):
                if not step.has(-1):
                    return
                par = step.parity_of(-1)
                pool.wait_ge(x1_summed, step.count(-1, GB, GB - 1))
                if step.positive(-3, 1, 0):
                    pool.wait_ge(stored[par], (step.loads(-3)) * GB)
                pool.tensor_tensor(res[:, par, :, :], x1[:, par, :, :],
                                   b2_rows[:, :].rearrange("p (a n) -> p a n", a=1).to_broadcast([P, GB, D]),
                                   ALU.add).then_inc(res_ready, 1)

            def edges_wait(step):
                if not step.has(1):
                    return
                pool.wait_ge(adj_loaded[step.parity_of(1)], step.loads(1))
                if step.positive(0, 1, 0):
                    pool.wait_ge(ebias_ready, step.count(0, 1, 0))

            def edges(step):
                if not step.has(1):
                    return
                par = step.parity_of(1)
                pool.tensor_scalar(absent[:, :, :], adj_in[:, par, :, :], 0.0, MASKED, ALU.is_le,
                                   ALU.mult).then_inc(absent_ready, 1)
                pool.tensor_scalar(adjf[:, :, :], adj_in[:, par, :, :], 1.0, None,
                                   ALU.mult).then_inc(adjf_ready, 1)
                pool.tensor_scalar(tenth[:, :, :], adj_in[:, par, :, :], 0.1, None,
                                   ALU.mult).then_inc(tenth_ready, 1)
                pool.wait_ge(adjf_ready, step.count(1, 1, 0))
                pool.wait_ge(tenth_ready, step.count(1, 1, 0))
                pool.tensor_tensor(tenth[:, :, :], tenth[:, :, :], adjf[:, :, :],
                                   ALU.mult).then_inc(square_ready, 1)
                pool.wait_ge(absent_ready, step.count(1, 1, 0))
                pool.wait_ge(square_ready, step.count(1, 1, 0))
                if step.positive(-1, GB, GB - 1):
                    pool.wait_ge(scores_taken, step.count(-1, GB, GB - 1))
                pool.tensor_tensor(ebias[:, par, :, :], tenth[:, :, :], absent[:, :, :],
                                   ALU.add).then_inc(ebias_ready, 1)

            pool.wait_ge(rows_loaded, 32)
            pool.wait_ge(bo_added, 1)
            pool.wait_ge(lo_made, 4)
            pool.wait_ge(hi_made, 4)

            def body(step):
                residual_start(step)
                rstd(step, 1, x_stats, mv1, ve1, x_veps, rstd1, x_rstd)
                rstd(step, -1, n_stats, mv2, ve2, n_veps, rstd2, n_rstd)
                edges_wait(step)
                result_start(step)
                edges(step)

            steps(pool, groups, body)


COLS = ["L0_gnn_ln1_g", "L0_gnn_ln1_b", "L0_gnn_ln2_g", "L0_gnn_ln2_b", "L0_gnn_bq", "L0_gnn_bk",
        "L0_gnn_bv", "L0_gnn_b1"]
INS = ["x", "adj", "cols", "L0_gnn_wq", "L0_gnn_wk", "L0_gnn_wv", "L0_gnn_wo", "L0_gnn_bo",
       "L0_gnn_w1", "L0_gnn_w2", "L0_gnn_b2"]


def lay_out(inputs):
    cols = np.concatenate([np.asarray(inputs[name]).reshape(-1, P).T for name in COLS], axis=1)
    return {name: np.ascontiguousarray(cols if name == "cols" else inputs[name]) for name in INS}


def build(nc, arrays):
    args = [nc.dram_tensor(f"in_{name}", arrays[name].shape, mybir.dt.from_np(arrays[name].dtype),
                           kind="ExternalInput").ap() for name in INS]
    out = nc.dram_tensor("out", arrays["x"].shape, F32, kind="ExternalOutput").ap()
    gnn_block(nc, *args, out)


def kernel(**inputs):
    import concourse.bacc as bacc
    from concourse.bass_utils import run_bass_kernel_spmd

    arrays = lay_out(inputs)
    nc = bacc.Bacc("TRN2", target_bir_lowering=False, num_devices=1)
    build(nc, arrays)
    feeds = {f"in_{name}": arrays[name] for name in INS}
    r = run_bass_kernel_spmd(nc, [feeds], core_ids=[0])
    return r.results[0]["out"]
```

```python
from contextlib import ExitStack

import numpy as np
import concourse.bass as bass
from concourse import mybir

F32 = mybir.dt.float32
F32R = mybir.dt.float32r
I32 = mybir.dt.int32
ALU = mybir.AluOpType
ACT = mybir.ActivationFunctionType
AX = mybir.AxisListType

P = 128
GB = 4
D = 256
DC = D // P
H = 8
HD = D // H
F = 1024
FC = F // P
RPB = P // HD
TOK = GB * P
VW = HD + 1
SCALE = 1.0 / float(np.sqrt(HD))
EPS = 1e-5
TERMS = 3
MOVES = TERMS * RPB
MASKED = -1e30

UNITS = ([("down", 0, -2), ("down", 1, -2)]
         + [("down", 2, -2), ("down", 3, -2)]
         + [("qk", 0, 1), ("qk", 1, 1), ("qk", 2, 1), ("qk", 3, 1)]
         + [("v", 0, 1), ("v", 1, 1)] + [("up", m, -1) for m in range(FC)])
PLACE = {(kind, i): at for at, (kind, i, _) in enumerate(UNITS)}
PER_GROUP = {"down": GB, "v": 2, "qk": 4, "up": FC}
assert len(UNITS) % 2 == 0


def column(parity, b):
    return b if parity else (b + 1) % GB


def first_place(parity):
    return 1 if parity else 0


def bank_of(kind, i):
    return PLACE[(kind, i)] % 2


class Step:

    def __init__(self, n, half, parity, groups, steady):
        self.n, self.half, self.parity, self.groups, self.steady = n, half, parity, groups, steady

    def has(self, off):
        return self.steady or 0 <= self.n + off < self.groups

    def parity_of(self, off):
        return (self.parity + off) % 2

    def has_graph(self, slot, back):
        return self.steady or 0 <= GB * self.n + slot - back < GB * self.groups

    def graphs(self, slot, back):
        return self.n * GB + (slot - back + 1)

    def count(self, off, per, i):
        return self.n * per + (off * per + i + 1)

    def loads(self, off):
        return self.half * 16 + ((self.parity + off) // 2 * 16 + 16)

    def positive(self, off, per, i):
        return self.steady or self.count(off, per, i) > 0


def steps(eng, groups, body):
    first, last = 2, groups - 2
    for n in range(-1, first):
        body(Step(n, n // 2, n % 2, groups, False))
    with eng.Fori(first // 2, last // 2) as i:
        for u in range(2):
            body(Step(i * 2 + u, i, u, groups, True))
    for n in range(last, groups + 2):
        body(Step(n, n // 2, n % 2, groups, False))


def gnn_block(nc, x, adj, cols, wq, wk, wv, wo, bo, w1, w2, b2, out):
    groups = x.shape[0] // GB
    assert x.shape[1] == P and x.shape[2] == D and groups % 2 == 0 and groups >= 6

    with ExitStack() as ctx:
        def sb(name, shape, dt=F32):
            return ctx.enter_context(nc.sbuf_tensor(name, shape, dt))

        def ps(name, shape):
            return ctx.enter_context(nc.psum_tensor(name, shape, F32))

        def sem(name):
            return ctx.enter_context(nc.semaphore(name))

        wa_hi = sb("wa_hi", [P, 4, DC, D], F32R)
        wa_lo = sb("wa_lo", [P, 4, DC, D], F32R)
        w1_hi = sb("w1_hi", [P, DC, F], F32R)
        w1_lo = sb("w1_lo", [P, DC, F], F32R)
        w2_hi = sb("w2_hi", [P, FC, D], F32R)
        w2_lo = sb("w2_lo", [P, FC, D], F32R)
        ident = sb("ident", [P, P])
        cols_in = sb("cols_in", [P, 7 * DC + FC])
        ln_cols = cols_in[:, 0:4 * DC].rearrange("p (j c) -> p j c", c=DC)
        bias_in = cols_in[:, 4 * DC:7 * DC].rearrange("p (j c) -> p j c", c=DC)
        b1_in = cols_in[:, 7 * DC:7 * DC + FC]
        bq_col = sb("bq_col", [P, DC])
        bv_col = sb("bv_col", [P, DC])
        g1_scaled = sb("g1_scaled", [P, DC])
        bqk_col = sb("bqk_col", [P, 2 * DC])
        b1_col = sb("b1_col", [P, FC])
        bv_wide = sb("bv_wide", [P, DC, P])
        bo_rows = sb("bo_rows", [P, D])
        b2_rows = sb("b2_rows", [P, D])

        xin = sb("xin", [P, 2, GB, D])
        x1 = sb("x1", [P, 2, GB, D])
        res = sb("res", [P, 2, GB, D])
        xhat = nhat = sb("xhat", [P, GB, D])
        xt_hi = sb("xt_hi", [P, DC, TOK], F32R)
        xt_lo = sb("xt_lo", [P, DC, TOK], F32R)
        nt_hi = sb("nt_hi", [P, DC, TOK], F32R)
        nt_lo = sb("nt_lo", [P, DC, TOK], F32R)
        stack = sb("stack", [P, RPB, 2, GB + 1, DC, P], F32R)
        vals = sb("vals", [P, 2, GB, H, VW])
        adj_in = sb("adj_in", [P, 2, GB, P], I32)
        ebias = sb("ebias", [P, 2, GB, P])
        tenth = sb("tenth", [P, GB, P])
        soft = sb("soft", [P, 2, H, P])
        sraw = soft[:, 0, :, :]
        prob = soft[:, 1, :, :]
        probt = sb("probt", [P, H, P])
        rmax = sb("rmax", [P, H])
        rsum = sb("rsum", [P, H])
        attn = sb("attn", [P, D])
        at_hi = sb("at_hi", [P, DC, P], F32R)
        at_lo = sb("at_lo", [P, DC, P], F32R)
        hid = sb("hid", [P, 3, TOK])
        hid_parts = sb("hid_parts", [P, FC, 2, TOK], F32R)
        hid_hi, hid_lo = hid_parts[:, :, 0, :], hid_parts[:, :, 1, :]
        st1 = sb("st1", [P, GB, 6])
        st2 = sb("st2", [P, GB, 6])
        mv1 = sb("mv1", [P, GB, 2])
        mv2 = sb("mv2", [P, GB, 2])
        ve1 = sb("ve1", [P, GB])
        ve2 = sb("ve2", [P, GB])
        rstd1 = sb("rstd1", [P, GB])
        rstd2 = sb("rstd2", [P, GB])
        mhalf = sb("mhalf", [P, GB])
        eps = sb("eps", [P, GB])
        gate = sb("gate", [P, 1])
        pool_gate = sb("pool_gate", [P, 1])
        w1_raw = res[:, :, :, :].rearrange("p a b n -> p (a b n)").rearrange("p (c n) -> p c n", c=DC)
        w2_raw = soft[:, :, :, :].rearrange("p a h k -> p (a h k)").rearrange("p (c n) -> p c n", c=FC)
        Q_LO, Q_HI, K_HI, K_LO = range(4)
        qk_parts = hid_parts[:, FC - 4:FC, :, :].rearrange("p m a t -> p (m a t)").rearrange(
            "p (k b c t) -> p k b c t", k=4, b=GB, c=DC)
        qk_hi = [qk_parts[:, k, :, c, :] for k in (Q_HI, K_HI) for c in range(DC)]
        qk_lo = [qk_parts[:, k, :, c, :] for k in (Q_LO, K_LO) for c in range(DC)]
        wa_raw = x1[:, :, :, :].rearrange("p a b n -> p (a b) n").rearrange(
            "p (a b) n -> p a b n", a=4)

        scores = ps("scores", [P, 2, 512])
        turned = ps("turned", [P, 2, 512])
        work = ps("work", [P, 2, 512])
        mixed = ps("mixed", [P, 512])
        wout = ps("wout", [P, 512])

        x_loaded = [sem("x_loaded0"), sem("x_loaded1")]
        adj_loaded = [sem("adj_loaded0"), sem("adj_loaded1")]
        stored = [sem("stored0"), sem("stored1")]
        cols_loaded = sem("cols_loaded")
        wa_loaded = [sem(f"wa_loaded{j}") for j in range(4)]
        w1_loaded = sem("w1_loaded")
        w2_loaded = sem("w2_loaded")
        rows_loaded = sem("rows_loaded")
        ident_clear = sem("ident_clear")
        ident_ready = sem("ident_ready")
        ones_set = sem("ones_set")
        mhalf_set = sem("mhalf_set")
        hi_made = sem("hi_made")
        lo_made = sem("lo_made")
        g1_ready = sem("g1_ready")
        qk_cols_ready = sem("qk_cols_ready")
        bq_ready = sem("bq_ready")
        bqk_ready = sem("bqk_ready")
        vb_cols_ready = sem("vb_cols_ready")
        bv_ready = sem("bv_ready")
        b1_ready = sem("b1_ready")
        bv_spread = sem("bv_spread")
        bo_ready = sem("bo_ready")
        bo_added = sem("bo_added")
        full = {k: sem(f"{k}_full") for k in (*PER_GROUP, "xt", "nt")}
        hi_taken = {k: sem(f"{k}_hi_taken") for k in ("xt", "nt")}
        taken = {k: sem(f"{k}_taken") for k in (*PER_GROUP, "xt", "nt")}
        x_stats = sem("x_stats")
        x_stat1 = sem("x_stat1")
        x_veps = sem("x_veps")
        x_rstd = sem("x_rstd")
        xhat_ready = sem("xhat_ready")
        n_stat1 = sem("n_stat1")
        n_stats = sem("n_stats")
        n_veps = sem("n_veps")
        n_rstd = sem("n_rstd")
        nhat_ready = sem("nhat_ready")
        x1_ready = sem("x1_ready")
        x1_summed = sem("x1_summed")
        res_ready = sem("res_ready")
        absent_ready = sem("absent_ready")
        adjf_ready = sem("adjf_ready")
        tenth_ready = sem("tenth_ready")
        square_ready = sem("square_ready")
        ebias_ready = sem("ebias_ready")
        qk_hi_ready = sem("qk_hi_ready")
        stacked = sem("stacked")
        scores_full = sem("scores_full")
        scores_taken = sem("scores_taken")
        max_ready = sem("max_ready")
        shifted = sem("shifted")
        prob_ready = sem("prob_ready")
        turned_full = sem("turned_full")
        turned_taken = sem("turned_taken")
        mixed_full = sem("mixed_full")
        sum_inverted = sem("sum_inverted")
        attn_ready = sem("attn_ready")
        at_full = sem("at_full")
        at_hi_taken = sem("at_hi_taken")
        at_taken = sem("at_taken")
        wout_full = sem("wout_full")
        hid_hi_ready = sem("hid_hi_ready")
        hid_lo_ready = sem("hid_lo_ready")

        x_g = x.rearrange("(g b) s d -> g s b d", b=GB)
        adj_g = adj.rearrange("(g b) q k -> g q b k", b=GB)
        out_g = out.rearrange("(g b) s d -> g s b d", b=GB)

        block = ctx.enter_context(nc.Block())

        @block.sync
        def _(sp):
            def group(step, off):
                return sp.snap(step.n + off) if step.steady else step.n + off

            def load(step, off, guard):
                if not step.has(off):
                    return
                par = step.parity_of(off)
                x_src, adj_src = x_g[group(step, off)], adj_g[group(step, off)]
                if guard:
                    sp.wait_ge(x1_ready, step.count(off - 2, 1, 0))
                sp.dma_start(xin[:, par, :, :], x_src).then_inc(x_loaded[par], 16)
                if guard:
                    sp.wait_ge(ebias_ready, step.count(off - 2, 1, 0))
                sp.dma_start(adj_in[:, par, :, :], adj_src).then_inc(adj_loaded[par], 16)

            start = Step(0, 0, 0, groups, False)
            chunked = "(c p) n -> p c n"
            sp.dma_start(cols_in[:, :], cols).then_inc(cols_loaded, 16)
            sp.dma_start(xin[:, 0, :, :], x_g[0]).then_inc(x_loaded[0], 16)
            for j, w in enumerate((wq, wk, wv, wo)):
                sp.dma_start(wa_raw[:, j, :, :], w.rearrange(chunked, p=P)).then_inc(wa_loaded[j], 16)
            sp.dma_start(adj_in[:, 0, :, :], adj_g[0]).then_inc(adj_loaded[0], 16)
            sp.dma_start(w1_raw, w1.rearrange(chunked, p=P)).then_inc(w1_loaded, 16)
            sp.dma_start(w2_raw, w2.rearrange(chunked, p=P)).then_inc(w2_loaded, 16)
            sp.dma_start(bo_rows[:, :], bo.rearrange("(a n) -> a n", a=1).to_broadcast([P, D])).then_inc(rows_loaded, 16)
            sp.dma_start(b2_rows[:, :], b2.rearrange("(a n) -> a n", a=1).to_broadcast([P, D])).then_inc(rows_loaded, 16)
            load(start, 1, False)

            def stack_terms(step):
                if not step.has(1):
                    return
                sp.wait_ge(taken["qk"], step.count(1, 4, 3))
                at = first_place(step.parity_of(1))
                for g in range(RPB):
                    r = slice(g * HD, (g + 1) * HD)
                    for term, (q, k) in enumerate(((Q_HI, K_HI), (Q_LO, K_HI), (Q_HI, K_LO))):
                        dst = stack[term * HD:(term + 1) * HD, g, :, at:at + GB, :, :]
                        sp.dma_start(dst.rearrange("p k b c t -> p k (b c t)").bitcast(F32),
                                     qk_parts[r, q:k + 1:k - q, :, :, :].rearrange(
                                         "p k b c t -> p k (b c t)").bitcast(F32)).then_inc(stacked, 16)

            def store(step, b):
                if step.has(-2):
                    par = step.parity_of(-2)
                    dst = out_g[group(step, -2)][:, b, :]
                    sp.wait_ge(taken["down"], step.count(-2, GB, b))
                    sp.dma_start(dst, res[:, par, b, :]).then_inc(stored[par], 16)

            def body(step):
                store(step, 0)
                store(step, 1)
                if step.has(0):
                    load(step, 2, True)
                store(step, 2)
                store(step, 3)
                stack_terms(step)

            steps(sp, groups, body)
            for par in range(2):
                sp.wait_ge(stored[par], 16 * GB * (groups // 2))

        @block.tensor
        def _(pe):
            def free(step, kind, i):
                at = PLACE[(kind, i)] - 2
                back = 0
                while True:
                    if at < 0:
                        at += len(UNITS)
                        back += 1
                    k, j, off = UNITS[at]
                    if step.has(off - back):
                        pe.wait_ge(taken[k], step.count(off - back, PER_GROUP[k], j))
                        return
                    if not step.steady and step.n - back < -2:
                        return
                    at -= 2

            def three(o, lhs_hi, lhs_lo, rhs_hi, rhs_lo, first, last):
                pe.matmul(o, lhs_hi, rhs_hi, start=first, stop=False)
                pe.matmul(o, lhs_hi, rhs_lo, start=False, stop=False)
                return pe.matmul(o, lhs_lo, rhs_hi, start=False, stop=last)

            def offset_column(o, w, off):
                for c in range(DC):
                    mm = pe.matmul(o, w[:, c, :], off[:, c:c + 1], start=(c == 0), stop=(c == DC - 1))
                return mm

            pe.wait_ge(cols_loaded, 16)
            for j in range(2):
                pe.wait_ge(wa_loaded[j], 16)
                for m in range(DC):
                    mm = offset_column(mixed[:, j * DC + m:j * DC + m + 1], wa_raw[:, j, :, m * P:(m + 1) * P],
                                ln_cols[:, 1, :])
            mm.then_inc(qk_cols_ready, 1)
            pe.wait_ge(ident_ready, 1)

            def late_columns():
                pe.wait_ge(wa_loaded[2], 16)
                for m in range(DC):
                    offset_column(wout[:, D + m:D + m + 1], wa_raw[:, 2, :, m * P:(m + 1) * P], ln_cols[:, 1, :])
                pe.wait_ge(w1_loaded, 16)
                for m in range(FC):
                    mm = offset_column(wout[:, D + DC + m:D + DC + m + 1], w1_raw[:, :, m * P:(m + 1) * P],
                                ln_cols[:, 3, :])
                mm.then_inc(vb_cols_ready, 1)

            def late_rows():
                pe.wait_ge(wa_loaded[3], 16)
                pe.wait_ge(bv_spread, 1)
                for c in range(DC):
                    mm = pe.matmul(wout[:, 0:D], bv_wide[:, c, :], wa_raw[:, 3, c, :],
                                   start=(c == 0), stop=(c == DC - 1))
                mm.then_inc(bo_ready, 1)

            def score(step, s):
                if not step.has_graph(s, 0) or not step.has(0):
                    return
                if s == 0:
                    pe.wait_ge(stacked, step.count(0, 1, 0) * (16 * MOVES))
                if step.has_graph(s, 1):
                    pe.wait_ge(scores_taken, step.graphs(s, 1))
                place = first_place(step.parity_of(0)) + column(step.parity_of(0), s)
                for h in range(H):
                    mm = pe.matmul(scores[:, h // RPB, (h % RPB) * P:(h % RPB + 1) * P],
                                   stack[0:TERMS * HD, h % RPB, 0, place, h // RPB, :],
                                   stack[0:TERMS * HD, h % RPB, 1, place, h // RPB, :], start=True, stop=True)
                mm.then_inc(scores_full, 1)

            def turn(step, s):
                if not step.has_graph(s, 1):
                    return
                pe.wait_ge(prob_ready, step.graphs(s, 1))
                if step.has_graph(s, 2):
                    pe.wait_ge(turned_taken, step.graphs(s, 2) * 2)
                for kind, slot, off in (("xt", 1, 1), ("nt", 2, -1)):
                    if s == slot + 1 and step.has(off):
                        pe.wait_ge(taken[kind], step.count(off, DC, DC - 1))
                for half in range(2):
                    for j in range(4):
                        mm = pe.transpose(turned[:, half, j * P:(j + 1) * P], prob[:, half * 4 + j, :],
                                          ident[:, :])
                    mm.then_inc(turned_full, 1)

            def mix(step, s):
                if not step.has_graph(s, 1):
                    return
                par = step.parity_of(-1 if s == 0 else 0)
                b = (s - 1) % GB
                pe.wait_ge(turned_taken, step.graphs(s, 1) * 2)
                if s == 1:
                    pe.wait_ge(taken["v"], step.count(0, 2, 1))
                if step.has_graph(s, 2):
                    pe.wait_ge(at_taken, step.graphs(s, 2))
                for h in range(H):
                    mm = pe.matmul(mixed[:, h * VW:(h + 1) * VW], probt[:, h, :],
                                   vals[:, par, b, h, :], start=True, stop=True)
                mm.then_inc(mixed_full, 1)

            def turn_attn(step, s):
                if not step.has_graph(s, 1):
                    return
                pe.wait_ge(attn_ready, step.graphs(s, 1))
                for c in range(DC):
                    mm = pe.transpose(mixed[:, c * P:(c + 1) * P], attn[:, c * P:(c + 1) * P], ident[:, :])
                mm.then_inc(at_full, 1)

            def project_out(step, s):
                if not step.has_graph(s, 2):
                    return
                if not step.steady and step.n == 0 and s == 2:
                    pe.wait_ge(lo_made, 7)
                    pe.wait_ge(bo_added, 1)
                pe.wait_ge(at_taken, step.graphs(s, 2))
                if step.has_graph(s, 3):
                    pe.wait_ge(x1_summed, step.graphs(s, 3))
                for c in range(DC):
                    mm = three(wout[:, 0:D], at_hi[:, c, :], at_lo[:, c, :], wa_hi[:, 3, c, :],
                               wa_lo[:, 3, c, :], c == 0, c == DC - 1)
                mm.then_inc(wout_full, 1)

            def flip(step, s, kind, c):
                off = 1 if kind == "xt" else -1
                if not step.has(off):
                    return
                src, ready = (xhat, xhat_ready) if kind == "xt" else (nhat, nhat_ready)
                if step.has_graph(s, 1):
                    pe.wait_ge(turned_taken, step.graphs(s, 1) * 2)
                for b in range(GB):
                    if c == 0:
                        pe.wait_ge(ready, step.count(off, GB, b))
                    at = column(step.parity_of(1), b) if kind == "xt" else b
                    mm = pe.transpose(turned[:, c, at * P:(at + 1) * P],
                                      src[:, b, c * P:(c + 1) * P], ident[:, :])
                mm.then_inc(full[kind], 1)

            def values(step, half):
                if not step.has(1):
                    return
                free(step, "v", half)
                if not step.steady and step.n == -1:
                    pe.wait_ge(lo_made, 3)
                for j in range(2):
                    at = column(step.parity_of(1), half * 2 + j)
                    cols = slice(at * P, (at + 1) * P)
                    for c in range(DC):
                        mm = three(work[:, bank_of("v", half), j * D:(j + 1) * D], xt_hi[:, c, cols],
                                   xt_lo[:, c, cols], wa_hi[:, 2, c, :], wa_lo[:, 2, c, :],
                                   c == 0, c == DC - 1)
                mm.then_inc(full["v"], 1)

            def query_key(step, m):
                if not step.has(1):
                    return
                free(step, "qk", m)
                if not step.steady and step.n == -1:
                    pe.wait_ge(lo_made, 1 + m // DC)
                if m == 0:
                    pe.wait_ge(taken["xt"], step.count(1, DC, DC - 1))
                w, cols = m // DC, slice((m % DC) * P, (m % DC + 1) * P)
                for c in range(DC):
                    mm = three(work[:, bank_of("qk", m), :], wa_hi[:, w, c, cols], wa_lo[:, w, c, cols],
                               xt_hi[:, c, :], xt_lo[:, c, :], c == 0, c == DC - 1)
                mm.then_inc(full["qk"], 1)

            def up(step, m):
                if not step.has(-1):
                    return
                free(step, "up", m)
                if m == 0:
                    pe.wait_ge(taken["nt"], step.count(-1, DC, DC - 1))
                cols = slice(m * P, (m + 1) * P)
                for c in range(DC):
                    mm = three(work[:, bank_of("up", m), :], w1_hi[:, c, cols], w1_lo[:, c, cols],
                               nt_hi[:, c, :], nt_lo[:, c, :], c == 0, c == DC - 1)
                mm.then_inc(full["up"], 1)

            def down(step, b):
                if not step.has(-2):
                    return
                free(step, "down", b)
                if b == 0:
                    pe.wait_ge(hid_lo_ready, step.count(-2, FC, FC - 4))
                cols = slice(b * P, (b + 1) * P)
                for m in range(FC):
                    if b == 0 and m >= FC - 3:
                        pe.wait_ge(hid_lo_ready, step.count(-2, FC, m))
                    mm = three(work[:, bank_of("down", b), 0:D], hid_hi[:, m, cols], hid_lo[:, m, cols],
                               w2_hi[:, m, :], w2_lo[:, m, :], m == 0, m == FC - 1)
                mm.then_inc(full["down"], 1)

            def body(step):
                score(step, 0)
                turn(step, 0)
                down(step, 0)
                project_out(step, 0)
                mix(step, 0)
                down(step, 1)
                turn_attn(step, 0)
                score(step, 1)
                turn(step, 1)
                down(step, 2)
                mix(step, 1)
                flip(step, 1, "xt", 0)
                project_out(step, 1)
                flip(step, 1, "xt", 1)
                down(step, 3)
                turn_attn(step, 1)
                score(step, 2)
                turn(step, 2)
                query_key(step, 0)
                query_key(step, 1)
                flip(step, 2, "nt", 0)
                flip(step, 2, "nt", 1)
                mix(step, 2)
                project_out(step, 2)
                query_key(step, 2)
                query_key(step, 3)
                turn_attn(step, 2)
                score(step, 3)
                turn(step, 3)
                values(step, 0)
                values(step, 1)
                project_out(step, 3)
                mix(step, 3)
                for m in range(FC):
                    up(step, m)
                turn_attn(step, 3)
                if not step.steady and step.n == -1:
                    late_columns()
                    late_rows()

            steps(pe, groups, body)

        @block.scalar
        def _(act):
            act.wait_ge(cols_loaded, 16)
            act.wait_ge(g1_ready, 1)
            for j in range(3):
                act.wait_ge(wa_loaded[j], 16)
                for c in range(DC):
                    gain = g1_scaled[:, c:c + 1] if j == 0 else ln_cols[:, 0, c:c + 1]
                    a = act.activation(wa_hi[:, j, c, :], wa_raw[:, j, c, :], ACT.Copy, scale=gain)
                a.then_inc(hi_made, 1)

            def late_hi(k):
                if k == 0:
                    act.wait_ge(wa_loaded[3], 16)
                    act.activation(wa_hi[:, 3, :, :], wa_raw[:, 3, :, :], ACT.Copy).then_inc(hi_made, 1)
                elif k <= DC:
                    act.wait_ge(w1_loaded, 16)
                    act.activation(w1_hi[:, k - 1, :], w1_raw[:, k - 1, :], ACT.Copy,
                                   scale=ln_cols[:, 2, k - 1:k]).then_inc(hi_made, 1)
                else:
                    act.wait_ge(w2_loaded, 16)
                    act.activation(w2_hi[:, :, :], w2_raw, ACT.Copy).then_inc(hi_made, 1)

            def turned_copy(step, s):
                if not step.has_graph(s, 1):
                    return
                for half in range(2):
                    act.wait_ge(turned_full, step.graphs(s, 1) * 2 + (half - 1))
                    act.activation(probt[:, half * 4:half * 4 + 4, :], turned[:, half, :].rearrange(
                        "p (h q) -> p h q", q=P), ACT.Copy).then_inc(turned_taken, 1)

            def exponential(step, s):
                if not step.has(0):
                    return
                act.wait_ge(shifted, step.graphs(s, 0))
                if step.has_graph(s, 1):
                    act.wait_ge(turned_full, step.graphs(s, 1) * 2)
                act.activation(prob[:, :, :], sraw[:, :, :], ACT.Exp).then_inc(prob_ready, 1)

            def attn_hi(step, s):
                if not step.has_graph(s, 1):
                    return
                act.wait_ge(at_full, step.graphs(s, 1))
                act.activation(at_hi[:, :, :], mixed[:, 0:D].rearrange("p (c q) -> p c q", c=DC),
                               ACT.Copy).then_inc(at_hi_taken, 1)

            def flip_hi(step, kind):
                off = 1 if kind == "xt" else -1
                if not step.has(off):
                    return
                dst = xt_hi if kind == "xt" else nt_hi
                for c in range(DC):
                    act.wait_ge(full[kind], step.count(off, DC, c))
                    act.activation(dst[:, c, :], turned[:, c, :], ACT.Copy)\
                       .then_inc(hi_taken[kind], 1)

            def values_copy(step, half):
                if not step.has(1):
                    return
                act.wait_ge(full["v"], step.count(1, 2, half))
                if not step.steady and step.n == -1:
                    act.wait_ge(ones_set, 1)
                act.activation(
                    vals[:, step.parity_of(1), half * 2:half * 2 + 2, :, 0:HD],
                    work[:, bank_of("v", half), :].rearrange("p (b h d) -> p b h d", b=2, h=H),
                    ACT.Copy).then_inc(taken["v"], 1)

            def query_key_copy(step, m):
                if not step.has(1):
                    return
                act.wait_ge(full["qk"], step.count(1, 4, m))
                if not step.steady and step.n == -1:
                    act.wait_ge(bqk_ready, 1)
                act.activation(qk_hi[m], work[:, bank_of("qk", m), :].rearrange("p (b t) -> p b t", b=GB),
                               ACT.Identity,
                               bias=bqk_col[:, m:m + 1]).then_inc(qk_hi_ready, 1)
                if not step.steady and step.n == -1:
                    late_hi(m)

            def gelu(step, m):
                if not step.has(-1):
                    return
                if step.positive(-1, FC, max(m - 3, -1)):
                    act.wait_ge(hid_lo_ready, step.count(-1, FC, max(m - 3, -1)))
                act.wait_ge(full["up"], step.count(-1, FC, m))
                if not step.steady and step.n == 1 and m == 0:
                    act.wait_ge(b1_ready, 1)
                act.activation(hid[:, m % 3, :], work[:, bank_of("up", m), :], ACT.Gelu,
                               bias=b1_col[:, m:m + 1]).then_inc(taken["up"], 1)

            def hidden_hi(step, m):
                if not step.has(-1):
                    return
                if m == FC - 4 and step.has(1):
                    act.wait_ge(stacked, step.count(1, 1, 0) * (16 * MOVES))
                act.wait_ge(taken["up"], step.count(-1, FC, m))
                act.activation(hid_hi[:, m, :], hid[:, m % 3, :], ACT.Copy).then_inc(hid_hi_ready, 1)

            def body(step):
                turned_copy(step, 0)
                exponential(step, 0)
                attn_hi(step, 0)
                turned_copy(step, 1)
                flip_hi(step, "xt")
                exponential(step, 1)
                attn_hi(step, 1)
                turned_copy(step, 2)
                query_key_copy(step, 0)
                query_key_copy(step, 1)
                flip_hi(step, "nt")
                exponential(step, 2)
                query_key_copy(step, 2)
                query_key_copy(step, 3)
                attn_hi(step, 2)
                turned_copy(step, 3)
                values_copy(step, 0)
                values_copy(step, 1)
                exponential(step, 3)
                for m in range(FC):
                    gelu(step, m)
                    if m >= 1:
                        hidden_hi(step, m - 1)
                hidden_hi(step, FC - 1)
                attn_hi(step, 3)

            steps(act, groups, body)

        @block.vector
        def _(dve):
            def setup():
                for j in range(3):
                    dve.wait_ge(hi_made, j + 1)
                    for c in range(DC):
                        gain = g1_scaled[:, c:c + 1] if j == 0 else ln_cols[:, 0, c:c + 1]
                        a = dve.scalar_tensor_tensor(wa_lo[:, j, c, :], wa_raw[:, j, c, :], gain,
                                                     wa_hi[:, j, c, :].bitcast(F32), ALU.mult, ALU.subtract)
                    a.then_inc(lo_made, 1)
                dve.wait_ge(qk_cols_ready, 1)
                dve.tensor_tensor(bq_col[:, :], mixed[:, 0:DC], bias_in[:, 0, :], ALU.add).then_inc(bq_ready, 1)
                dve.tensor_tensor(bqk_col[:, DC:2 * DC], mixed[:, DC:2 * DC], bias_in[:, 1, :],
                                  ALU.add).then_inc(bq_ready, 1)
                dve.wait_ge(bq_ready, 2)
                dve.tensor_scalar(bqk_col[:, 0:DC], bq_col[:, :], SCALE, None, ALU.mult).then_inc(bqk_ready, 1)
                dve.wait_ge(bqk_ready, 1)

            def late_lo(k):
                dve.wait_ge(hi_made, 4 + k)
                if k == 0:
                    a = dve.tensor_tensor(wa_lo[:, 3, :, :], wa_raw[:, 3, :, :],
                                          wa_hi[:, 3, :, :].bitcast(F32), ALU.subtract)
                elif k <= DC:
                    a = dve.scalar_tensor_tensor(w1_lo[:, k - 1, :], w1_raw[:, k - 1, :],
                                                 ln_cols[:, 2, k - 1:k], w1_hi[:, k - 1, :].bitcast(F32),
                                                 ALU.mult, ALU.subtract)
                else:
                    a = dve.tensor_tensor(w2_lo[:, :, :], w2_raw, w2_hi[:, :, :].bitcast(F32), ALU.subtract)
                a.then_inc(lo_made, 1)

            def late_biases():
                dve.wait_ge(vb_cols_ready, 1)
                dve.tensor_tensor(bv_col[:, :], wout[:, D:D + DC], bias_in[:, 2, :], ALU.add)\
                   .then_inc(bv_ready, 1)
                dve.tensor_tensor(b1_col[:, :], wout[:, D + DC:D + DC + FC], b1_in, ALU.add)\
                   .then_inc(b1_ready, 1)
                dve.wait_ge(bv_ready, 1)
                dve.tensor_copy(bv_wide[:, :, :], bv_col[:, :].rearrange("p (c a) -> p c a", a=1)
                                .to_broadcast([P, DC, P])).then_inc(bv_spread, 1)

            def late_rows():
                dve.wait_ge(rows_loaded, 32)
                dve.wait_ge(bo_ready, 1)
                dve.tensor_tensor(bo_rows[:, :], wout[:, 0:D], bo_rows[:, :], ALU.add).then_inc(bo_added, 1)

            def softmax(step, s):
                if not step.has(0):
                    return
                par = step.parity_of(0)
                if not step.steady and step.n == 0 and s == 0:
                    dve.wait_ge(lo_made, 7)
                dve.wait_ge(scores_full, step.graphs(s, 0))
                if s == 0:
                    dve.wait_ge(ebias_ready, step.count(0, 1, 0))
                if step.has_graph(s, 1):
                    dve.wait_ge(prob_ready, step.graphs(s, 1))
                edge = ebias[:, par, s, :].rearrange("p (a k) -> p a k", a=1).to_broadcast([P, H, P])
                dve.tensor_tensor(sraw[:, :, :], scores[:, :, :].rearrange("p t (h k) -> p (t h) k", k=P),
                                  edge, ALU.add).then_inc(scores_taken, 1)
                dve.wait_ge(scores_taken, step.graphs(s, 0))
                dve.tensor_reduce(rmax[:, :], sraw[:, :, :], AX.X, ALU.max).then_inc(max_ready, 1)
                dve.wait_ge(max_ready, step.graphs(s, 0))
                dve.tensor_tensor(sraw[:, :, :], sraw[:, :, :],
                                  rmax[:, :].rearrange("p (h a) -> p h a", a=1).to_broadcast([P, H, P]),
                                  ALU.subtract).then_inc(shifted, 1)

            def normalise(step, s):
                if not step.has_graph(s, 1):
                    return
                dve.wait_ge(mixed_full, step.graphs(s, 1))
                heads = mixed[:, 0:H * VW].rearrange("p (h d) -> p h d", d=VW)
                dve.reciprocal(rsum[:, :].rearrange("p (h a) -> p h a", a=1),
                               heads[:, :, HD:VW]).then_inc(sum_inverted, 1)
                dve.wait_ge(sum_inverted, step.graphs(s, 1))
                dve.tensor_tensor(attn[:, :].rearrange("p (h d) -> p h d", d=HD), heads[:, :, 0:HD],
                                  rsum[:, :].rearrange("p (h a) -> p h a", a=1).to_broadcast([P, H, HD]),
                                  ALU.mult).then_inc(attn_ready, 1)

            def attn_lo(step, s):
                if not step.has_graph(s, 1):
                    return
                dve.wait_ge(at_hi_taken, step.graphs(s, 1))
                dve.tensor_tensor(at_lo[:, :, :], mixed[:, 0:D].rearrange("p (c q) -> p c q", c=DC),
                                  at_hi[:, :, :].bitcast(F32), ALU.subtract).then_inc(at_taken, 1)

            def residual(step, s):
                if not step.has_graph(s, 2):
                    return
                b = (s - 2) % GB
                off = -1 if s < 2 else 0
                par = step.parity_of(off)
                if b == 0:
                    dve.wait_ge(x1_ready, step.count(off, 1, 0))
                dve.wait_ge(wout_full, step.graphs(s, 2))
                dve.tensor_tensor(x1[:, par, b, :], wout[:, 0:D], x1[:, par, b, :],
                                  ALU.add).then_inc(x1_summed, 1)
                dve.wait_ge(x1_summed, step.graphs(s, 2))
                dve.bn_stats(st2[:, b, :], x1[:, par, b, :]).then_inc(n_stat1, 1)
                if b == GB - 1:
                    dve.wait_ge(n_stat1, step.graphs(s, 2))
                    dve.memset(gate[:, :], 0.0)
                    for j in range(GB):
                        a = dve.bn_aggr(mv2[:, j, :], st2[:, j, :])
                    a.then_inc(n_stats, 1)

            def stats1(step):
                if not step.has(1):
                    return
                par = step.parity_of(1)
                dve.wait_ge(x_loaded[par], step.loads(1))
                for b in range(GB):
                    a = dve.bn_stats(st1[:, b, :], xin[:, par, b, :])
                a.then_inc(x_stat1, 1)
                dve.wait_ge(x_stat1, step.count(1, 1, 0))
                dve.memset(gate[:, :], 0.0)
                for b in range(GB):
                    a = dve.bn_aggr(mv1[:, b, :], st1[:, b, :])
                a.then_inc(x_stats, 1)

            def norm1(step):
                if not step.has(1):
                    return
                par = step.parity_of(1)
                dve.wait_ge(x_rstd, step.count(1, 1, 0))
                if step.positive(0, DC, DC - 1):
                    dve.wait_ge(full["xt"], step.count(0, DC, DC - 1))
                if step.positive(-2, DC, DC - 1):
                    dve.wait_ge(full["nt"], step.count(-2, DC, DC - 1))
                for b in range(GB):
                    dve.tensor_scalar(xhat[:, b, :], xin[:, par, b, :], mv1[:, b, 0:1], rstd1[:, b:b + 1],
                                      ALU.subtract, ALU.mult).then_inc(xhat_ready, 1)

            def norm2(step):
                if not step.has(-1):
                    return
                par = step.parity_of(-1)
                dve.wait_ge(n_rstd, step.count(-1, 1, 0))
                if step.has(1):
                    dve.wait_ge(full["xt"], step.count(1, DC, DC - 1))
                for b in range(GB):
                    dve.tensor_scalar(nhat[:, b, :], x1[:, par, b, :], mv2[:, b, 0:1], rstd2[:, b:b + 1],
                                      ALU.subtract, ALU.mult).then_inc(nhat_ready, 1)

            def flip_lo(step, kind):
                off = 1 if kind == "xt" else -1
                if not step.has(off):
                    return
                hi, lo = (xt_hi, xt_lo) if kind == "xt" else (nt_hi, nt_lo)
                for c in range(DC):
                    dve.wait_ge(hi_taken[kind], step.count(off, DC, c))
                    dve.tensor_tensor(lo[:, c, :], turned[:, c, :], hi[:, c, :].bitcast(F32),
                                      ALU.subtract).then_inc(taken[kind], 1)

            def query_key_lo(step, m):
                if not step.has(1):
                    return
                dve.wait_ge(qk_hi_ready, step.count(1, 4, m))
                dve.scalar_tensor_tensor(qk_lo[m], work[:, bank_of("qk", m), :].rearrange(
                    "p (b t) -> p b t", b=GB), bqk_col[:, m:m + 1],
                                         qk_hi[m].bitcast(F32), ALU.add, ALU.subtract)\
                   .then_inc(taken["qk"], 1)
                if not step.steady and step.n == -1:
                    late_lo(m)

            def hidden_lo(step, m):
                if not step.has(-1):
                    return
                dve.wait_ge(hid_hi_ready, step.count(-1, FC, m))
                dve.tensor_tensor(hid_lo[:, m, :], hid[:, m % 3, :], hid_hi[:, m, :].bitcast(F32),
                                  ALU.subtract).then_inc(hid_lo_ready, 1)

            def result(step, b):
                if not step.has(-2):
                    return
                par = step.parity_of(-2)
                if b == 0:
                    dve.wait_ge(res_ready, step.count(-2, 1, 0))
                dve.wait_ge(full["down"], step.count(-2, GB, b))
                dve.tensor_tensor(res[:, par, b, :], work[:, bank_of("down", b), 0:D],
                                  res[:, par, b, :], ALU.add).then_inc(taken["down"], 1)

            def body(step):
                first = not step.steady and step.n == -1
                softmax(step, 0)
                result(step, 0)
                residual(step, 0)
                normalise(step, 0)
                stats1(step)
                result(step, 1)
                attn_lo(step, 0)
                norm1(step)
                if first:
                    setup()
                softmax(step, 1)
                result(step, 2)
                normalise(step, 1)
                residual(step, 1)
                flip_lo(step, "xt")
                result(step, 3)
                attn_lo(step, 1)
                norm2(step)
                softmax(step, 2)
                query_key_lo(step, 0)
                query_key_lo(step, 1)
                normalise(step, 2)
                flip_lo(step, "nt")
                residual(step, 2)
                query_key_lo(step, 2)
                query_key_lo(step, 3)
                attn_lo(step, 2)
                softmax(step, 3)
                normalise(step, 3)
                residual(step, 3)
                for m in range(FC):
                    hidden_lo(step, m)
                attn_lo(step, 3)
                if first:
                    late_biases()
                    late_rows()

            dve.memset(vals[:, :, :, :, HD:VW], 1.0).then_inc(ones_set, 1)
            dve.wait_ge(cols_loaded, 16)
            dve.tensor_scalar(g1_scaled[:, :], ln_cols[:, 0, :], SCALE, None, ALU.mult).then_inc(g1_ready, 1)
            dve.wait_ge(g1_ready, 1)
            steps(dve, groups, body)

        @block.gpsimd
        def _(pool):
            pool.memset(ident[:, :], 0.0).then_inc(ident_clear, 1)
            pool.wait_ge(ident_clear, 1)
            pool.affine_select(out=ident[:, :], in_=ident[:, :], compare_op=ALU.not_equal, fill=1.0,
                               base=0, pattern=[[-1, P]], channel_multiplier=1).then_inc(ident_ready, 1)
            pool.memset(mhalf[:, :], -0.5).then_inc(mhalf_set, 1)
            pool.memset(eps[:, :], EPS).then_inc(mhalf_set, 1)
            pool.wait_ge(mhalf_set, 2)

            def rstd(step, off, stats, mv, ve, veps, o, done):
                if not step.has(off):
                    return
                pool.wait_ge(stats, step.count(off, 1, 0))
                pool.tensor_tensor(ve[:, :], mv[:, :, 1:2].rearrange("p b a -> p (b a)"), eps[:, :],
                                   ALU.add).then_inc(veps, 1)
                pool.wait_ge(veps, step.count(off, 1, 0))
                pool.tensor_tensor(o[:, :], ve[:, :], mhalf[:, :], ALU.pow).then_inc(done, 1)

            def residual_start(step):
                if not step.has(0):
                    return
                par = step.parity_of(0)
                if not step.steady and step.n == 0:
                    pool.wait_ge(rows_loaded, 32)
                    pool.wait_ge(bo_added, 1)
                pool.wait_ge(x_loaded[par], step.loads(0))
                pool.wait_ge(xhat_ready, step.count(0, GB, GB - 1))
                if step.positive(-2, 1, 0):
                    pool.wait_ge(nhat_ready, step.count(-2, GB, GB - 1))
                    pool.wait_ge(res_ready, step.count(-2, 1, 0))
                pool.tensor_tensor(x1[:, par, :, :], xin[:, par, :, :],
                                   bo_rows[:, :].rearrange("p (a n) -> p a n", a=1).to_broadcast([P, GB, D]),
                                   ALU.add).then_inc(x1_ready, 1)

            def result_start(step):
                if not step.has(-1):
                    return
                par = step.parity_of(-1)
                pool.wait_ge(x1_summed, step.count(-1, GB, GB - 1))
                if step.positive(-3, 1, 0):
                    pool.wait_ge(stored[par], (step.loads(-3)) * GB)
                pool.tensor_tensor(res[:, par, :, :], x1[:, par, :, :],
                                   b2_rows[:, :].rearrange("p (a n) -> p a n", a=1).to_broadcast([P, GB, D]),
                                   ALU.add).then_inc(res_ready, 1)

            def edges_wait(step):
                if not step.has(1):
                    return
                pool.wait_ge(adj_loaded[step.parity_of(1)], step.loads(1))
                if step.positive(0, 1, 0):
                    pool.wait_ge(ebias_ready, step.count(0, 1, 0))
                if step.positive(-1, GB, GB - 1):
                    pool.wait_ge(scores_taken, step.count(-1, GB, GB - 1))

            def edges(step):
                if not step.has(1):
                    return
                par = step.parity_of(1)
                numbers, whole = adj_in[:, par, :, :], adj_in[:, par, :, :].bitcast(F32)
                pool.tensor_scalar(tenth[:, :, :], numbers, 0.1, None, ALU.mult).then_inc(tenth_ready, 1)
                pool.tensor_scalar(ebias[:, par, :, :], numbers, 0.0, MASKED, ALU.is_le,
                                   ALU.mult).then_inc(absent_ready, 1)
                pool.wait_ge(absent_ready, step.count(1, 1, 0))
                pool.wait_ge(tenth_ready, step.count(1, 1, 0))
                pool.tensor_tensor(pool_gate[:, :], eps[:, 0:1], eps[:, 0:1], ALU.add)
                pool.tensor_scalar(whole, numbers, 1.0, None, ALU.mult).then_inc(adjf_ready, 1)
                pool.wait_ge(adjf_ready, step.count(1, 1, 0))
                pool.tensor_tensor(tenth[:, :, :], tenth[:, :, :], whole, ALU.mult).then_inc(square_ready, 1)
                pool.wait_ge(square_ready, step.count(1, 1, 0))
                pool.tensor_tensor(ebias[:, par, :, :], tenth[:, :, :], ebias[:, par, :, :],
                                   ALU.add).then_inc(ebias_ready, 1)

            def body(step):
                if step.steady or step.n != 0:
                    residual_start(step)
                rstd(step, 1, x_stats, mv1, ve1, x_veps, rstd1, x_rstd)
                if not step.steady and step.n == 0:
                    residual_start(step)
                rstd(step, -1, n_stats, mv2, ve2, n_veps, rstd2, n_rstd)
                edges_wait(step)
                result_start(step)
                edges(step)

            steps(pool, groups, body)


COLS = ["L0_gnn_ln1_g", "L0_gnn_ln1_b", "L0_gnn_ln2_g", "L0_gnn_ln2_b", "L0_gnn_bq", "L0_gnn_bk",
        "L0_gnn_bv", "L0_gnn_b1"]
INS = ["x", "adj", "cols", "L0_gnn_wq", "L0_gnn_wk", "L0_gnn_wv", "L0_gnn_wo", "L0_gnn_bo",
       "L0_gnn_w1", "L0_gnn_w2", "L0_gnn_b2"]


def lay_out(inputs):
    cols = np.concatenate([np.asarray(inputs[name]).reshape(-1, P).T for name in COLS], axis=1)
    return {name: np.ascontiguousarray(cols if name == "cols" else inputs[name]) for name in INS}


def build(nc, arrays):
    args = [nc.dram_tensor(f"in_{name}", arrays[name].shape, mybir.dt.from_np(arrays[name].dtype),
                           kind="ExternalInput").ap() for name in INS]
    out = nc.dram_tensor("out", arrays["x"].shape, F32, kind="ExternalOutput").ap()
    gnn_block(nc, *args, out)


def kernel(**inputs):
    import concourse.bacc as bacc
    from concourse.bass_utils import run_bass_kernel_spmd

    arrays = lay_out(inputs)
    nc = bacc.Bacc("TRN2", target_bir_lowering=False, num_devices=1)
    build(nc, arrays)
    feeds = {f"in_{name}": arrays[name] for name in INS}
    r = run_bass_kernel_spmd(nc, [feeds], core_ids=[0])
    return r.results[0]["out"]
```
